# Optimizing a Trainium2 kernel written in Bass

```python
import numpy as np
import jax
import jax.numpy as jnp

def _softmax(x, axis=-1):
    return jax.nn.softmax(x, axis=axis)

def _gelu(x):
    return jax.nn.gelu(x, approximate=True)

def _silu(x):
    return jax.nn.silu(x)

def _sigmoid(x):
    return jax.nn.sigmoid(x)

def _layernorm(x, axis=-1, eps=1e-05):
    m = jnp.mean(x, axis=axis, keepdims=True)
    v = jnp.var(x, axis=axis, keepdims=True)
    return (x - m) / jnp.sqrt(v + eps)

def _scatter_add(tgt, idx, src, axis=0):
    return tgt.at[idx].add(src)

def _segment_sum(src, seg, n):
    return jax.ops.segment_sum(src, seg, n)
kernel_name = 'mk_gps_d1_gnn_r8_85a073'

def setup_inputs(seed: int=0):
    np.random.seed(seed)
    _w = jnp.asarray

    def _rec_inputs():
        import jax
        import jax.numpy as jnp
        _gk = jax.random.key(seed)
        x = -6.415e-05 + 1 * jax.random.normal(jax.random.fold_in(_gk, 1), (1250, 1024), jnp.float32)
        _s = jax.random.randint(jax.random.fold_in(_gk, 2), (20000,), 0, 1250, jnp.int32)
        _d = jax.random.randint(jax.random.fold_in(_gk, 3), (20000,), 0, 1250, jnp.int32)
        _loop = jnp.arange(1250, dtype=jnp.int32)
        src = jnp.concatenate([_s, _d, _loop])
        dst = jnp.concatenate([_d, _s, _loop])
        _o = jnp.argsort(dst, stable=True)
        src = src[_o]
        dst = dst[_o]
        return (x, src, dst)
    x, src, dst = _rec_inputs()

    def _L0_gnn_setup():
        import jax, jax.numpy as jnp
        import numpy as np
        N_NODES = 1250
        N_EDGES = 20000
        DIM = 1024
        key = jax.random.key(seed)
        k1, k2, k3 = jax.random.split(key, 3)
        x = jax.random.normal(k1, (N_NODES, DIM), dtype=jnp.float32)
        edge_index = jax.random.randint(k2, (2, N_EDGES), 0, N_NODES, dtype=jnp.int64)
        W = jax.random.normal(k3, (DIM, DIM), dtype=jnp.float32) * (1.0 / np.sqrt(DIM))
        b = jnp.zeros((DIM,), dtype=jnp.float32)
        return {'x': x, 'edge_index': edge_index, 'W': W, 'b': b}
    _L0_gnn_all = _L0_gnn_setup()
    _L0_gnn_in = {k: v for k, v in _L0_gnn_all.items() if k in ('W', 'b')}
    del _L0_gnn_all

    def _L0_mix_setup():
        import jax, jax.numpy as jnp
        import numpy as np
        NUM_HEADS = 16
        EPS = 1e-06

        def elu_plus_one(x):
            return jax.nn.elu(x) + 1.0
        key = jax.random.key(seed)
        ks = jax.random.split(key, 9)
        B, L, E = (4, 512, 1024)
        s = 1.0 / np.sqrt(E)
        return {'query': jax.random.normal(ks[0], (B, L, E), jnp.float32), 'Wq': jax.random.normal(ks[1], (E, E), jnp.float32) * s, 'bq': jax.random.normal(ks[2], (E,), jnp.float32) * 0.01, 'Wk': jax.random.normal(ks[3], (E, E), jnp.float32) * s, 'bk': jax.random.normal(ks[4], (E,), jnp.float32) * 0.01, 'Wv': jax.random.normal(ks[5], (E, E), jnp.float32) * s, 'bv': jax.random.normal(ks[6], (E,), jnp.float32) * 0.01, 'Wo': jax.random.normal(ks[7], (E, E), jnp.float32) * s, 'bo': jax.random.normal(ks[8], (E,), jnp.float32) * 0.01}
    _L0_mix_all = _L0_mix_setup()
    _L0_mix_in = {k: v for k, v in _L0_mix_all.items() if k in ('Wq', 'bq', 'Wk', 'bk', 'Wv', 'bv', 'Wo', 'bo')}
    del _L0_mix_all

    def _L0_ffn_setup():
        import jax, jax.numpy as jnp
        import numpy as np
        D_IN, D_HID = (1024, 512)

        def _ternary(key, shape):
            return jax.random.randint(key, shape, -1, 2).astype(jnp.float32)

        def _tlin(x, w, s):
            return jnp.einsum('bsi,oi->bso', x, w) * s
        key = jax.random.key(seed)
        ks = jax.random.split(key, 12)
        inv = lambda fan: 1.0 / np.sqrt(fan).astype(np.float32)
        return {'x': jax.random.normal(ks[0], (4, 256, D_IN), dtype=jnp.float32), 'w1_w': _ternary(ks[1], (D_HID, D_IN)), 'w1_s': jax.random.uniform(ks[2], (D_HID,), dtype=jnp.float32) * inv(D_IN), 'w2_w': _ternary(ks[3], (D_HID, D_IN)), 'w2_s': jax.random.uniform(ks[4], (D_HID,), dtype=jnp.float32) * inv(D_IN), 'h1_w': _ternary(ks[5], (D_HID, D_HID)), 'h1_s': jax.random.uniform(ks[6], (D_HID,), dtype=jnp.float32) * inv(D_HID), 'h2_w': _ternary(ks[7], (D_HID, D_HID)), 'h2_s': jax.random.uniform(ks[8], (D_HID,), dtype=jnp.float32) * inv(D_HID), 'w3_w': _ternary(ks[9], (D_IN, D_HID)), 'w3_s': jax.random.uniform(ks[10], (D_IN,), dtype=jnp.float32) * inv(D_HID)}
    _L0_ffn_all = _L0_ffn_setup()
    _L0_ffn_in = {k: v for k, v in _L0_ffn_all.items() if k in ('w1_w', 'w1_s', 'w2_w', 'w2_s', 'h1_w', 'h1_s', 'h2_w', 'h2_s', 'w3_w', 'w3_s')}
    del _L0_ffn_all
    return {'x': x, 'src': src, 'dst': dst, 'L0_gnn_W': _L0_gnn_in['W'], 'L0_gnn_b': _L0_gnn_in['b'], 'L0_mix_Wq': _L0_mix_in['Wq'], 'L0_mix_bq': _L0_mix_in['bq'], 'L0_mix_Wk': _L0_mix_in['Wk'], 'L0_mix_bk': _L0_mix_in['bk'], 'L0_mix_Wv': _L0_mix_in['Wv'], 'L0_mix_bv': _L0_mix_in['bv'], 'L0_mix_Wo': _L0_mix_in['Wo'], 'L0_mix_bo': _L0_mix_in['bo'], 'L0_ffn_w1_w': _L0_ffn_in['w1_w'], 'L0_ffn_w1_s': _L0_ffn_in['w1_s'], 'L0_ffn_w2_w': _L0_ffn_in['w2_w'], 'L0_ffn_w2_s': _L0_ffn_in['w2_s'], 'L0_ffn_h1_w': _L0_ffn_in['h1_w'], 'L0_ffn_h1_s': _L0_ffn_in['h1_s'], 'L0_ffn_h2_w': _L0_ffn_in['h2_w'], 'L0_ffn_h2_s': _L0_ffn_in['h2_s'], 'L0_ffn_w3_w': _L0_ffn_in['w3_w'], 'L0_ffn_w3_s': _L0_ffn_in['w3_s']}

def reference(x, src, dst, L0_gnn_W, L0_gnn_b, L0_mix_Wq, L0_mix_bq, L0_mix_Wk, L0_mix_bk, L0_mix_Wv, L0_mix_bv, L0_mix_Wo, L0_mix_bo, L0_ffn_w1_w, L0_ffn_w1_s, L0_ffn_w2_w, L0_ffn_w2_s, L0_ffn_h1_w, L0_ffn_h1_s, L0_ffn_h2_w, L0_ffn_h2_s, L0_ffn_w3_w, L0_ffn_w3_s):
    import jax
    import jax.numpy as jnp

    def _L0_gnn_ref(x, edge_index, W, b):
        import jax, jax.numpy as jnp
        import numpy as np
        N_NODES = 1250
        N_EDGES = 20000
        DIM = 1024
        'GCNConv (add_self_loops=True, symmetric norm) -> Dropout(eval=identity) -> ReLU.'
        n = x.shape[0]
        loops = jnp.arange(n, dtype=edge_index.dtype)
        src = jnp.concatenate([edge_index[0], loops])
        dst = jnp.concatenate([edge_index[1], loops])
        deg = jax.ops.segment_sum(jnp.ones_like(dst, dtype=x.dtype), dst, num_segments=n)
        dinv = jnp.where(deg > 0, jax.lax.rsqrt(deg), jnp.zeros_like(deg))
        norm = dinv[src] * dinv[dst]
        h = x @ W
        msg = h[src] * norm[:, None]
        out = jax.ops.segment_sum(msg, dst, num_segments=n) + b
        return jax.nn.relu(out)

    def _L0_mix_ref(query, Wq, bq, Wk, bk, Wv, bv, Wo, bo):
        import jax, jax.numpy as jnp
        import numpy as np
        NUM_HEADS = 16
        EPS = 1e-06

        def elu_plus_one(x):
            return jax.nn.elu(x) + 1.0
        B, L, E = query.shape
        H = NUM_HEADS
        d = E // H

        def proj(x, W, b):
            return jnp.einsum('ble,fe->blf', x, W) + b

        def heads(x):
            return x.reshape(B, L, H, d).transpose(0, 2, 1, 3)
        Q = heads(proj(query, Wq, bq))
        K = heads(proj(query, Wk, bk))
        V = heads(proj(query, Wv, bv))
        phiQ = elu_plus_one(Q)
        phiK = elu_plus_one(K)
        S = jnp.einsum('bhki,bhkj->bhij', phiK, V)
        Z = phiK.sum(axis=-2)
        num = jnp.einsum('bhqi,bhij->bhqj', phiQ, S)
        denom = jnp.einsum('bhqi,bhi->bhq', phiQ, Z)[..., None] + EPS
        context = (num / denom).transpose(0, 2, 1, 3).reshape(B, L, E)
        return jnp.einsum('ble,fe->blf', context, Wo) + bo

    def _L0_ffn_ref(x, w1_w, w1_s, w2_w, w2_s, h1_w, h1_s, h2_w, h2_s, w3_w, w3_s):
        import jax, jax.numpy as jnp
        import numpy as np
        D_IN, D_HID = (1024, 512)

        def _ternary(key, shape):
            return jax.random.randint(key, shape, -1, 2).astype(jnp.float32)

        def _tlin(x, w, s):
            return jnp.einsum('bsi,oi->bso', x, w) * s
        h = jax.nn.silu(_tlin(x, w1_w, w1_s)) * _tlin(x, w2_w, w2_s)
        h = jax.nn.gelu(_tlin(h, h1_w, h1_s), approximate=False)
        h = jax.nn.gelu(_tlin(h, h2_w, h2_s), approximate=False)
        return _tlin(h, w3_w, w3_s)
    edge_index = jnp.stack([src, dst])
    xn = _layernorm(x, axis=-1)
    x = x + _L0_gnn_ref(xn, edge_index, L0_gnn_W, L0_gnn_b) + _L0_mix_ref(xn[None], L0_mix_Wq, L0_mix_bq, L0_mix_Wk, L0_mix_bk, L0_mix_Wv, L0_mix_bv, L0_mix_Wo, L0_mix_bo)[0]
    x = x + _L0_ffn_ref(_layernorm(x, axis=-1)[None], L0_ffn_w1_w, L0_ffn_w1_s, L0_ffn_w2_w, L0_ffn_w2_s, L0_ffn_h1_w, L0_ffn_h1_s, L0_ffn_h2_w, L0_ffn_h2_s, L0_ffn_w3_w, L0_ffn_w3_s)[0]
    return x

_drawn_inputs = setup_inputs


def setup_inputs(seed=0):
    import zlib

    import numpy as np

    out = dict(_drawn_inputs(seed))
    spreads = {'L0_gnn_b': (0.0, 0.1)}
    factors = {}
    for name, (base, spread) in spreads.items():
        noise = np.random.default_rng([zlib.crc32(name.encode()), seed]).standard_normal(out[name].shape)
        drawn = base * np.exp(spread * noise) if base else spread * noise
        out[name] = jnp.asarray(drawn.astype(out[name].dtype))
    for name, factor in factors.items():
        out[name] = (out[name] * factor).astype(out[name].dtype)
    return out
```

```python
from contextlib import ExitStack

import concourse.bass as bass
from concourse import mybir

F32 = mybir.dt.float32
F32R = mybir.dt.float32r
BF16 = mybir.dt.bfloat16
F16 = mybir.dt.float16
I32 = mybir.dt.int32
U16 = mybir.dt.uint16
ALU = mybir.AluOpType
ACT = mybir.ActivationFunctionType
AX = mybir.AxisListType
RMAX = bass.bass_isa.ReduceOp.max

P = 128
N = 1250
D = 1024
HID = 512
E = 41250
NT = -(-N // P)
KD = D // P
KH = HID // P
HALF = 512
NCH = -(-E // P)
ROWS_P, ROWS_T = 108, 3
NCH_PAD = 336
STATIC_CHUNKS = 6
EXTRA_CHUNKS = 2
WIN = 16
WCOLS = WIN * NT
NWIN = NT * P // WIN
WPT = P // WIN
CHUNKS = [(0, 418), (418, 416), (834, 416)]
RING = 10
STAGE = 3
EXACT_COUNT = 4096
LN_EPS = 1e-5
DEN_EPS = 1e-6
NEVER = 4095
BIG = 400.0

KV0, Q0, G0, M0, A0, B0, C0, D0, E0 = 0, 32, 48, 64, 72, 80, 88, 92, 96
NSLICE = 104


GATED = [(2 * s + f, c) for s in range(2) for c in range(3) for f in range(2)]


def rows(t):
    return min(P, N - t * P)


def units():
    u = [("kv", s, t) for s in range(4) for t in range(NT)]
    u += [("z", i) for i in range(2)]
    u += [("q", f, c) for f in range(KD) for c in range(3)]
    u += [("h", 0, t) for t in range(NT)]
    u += [("agg", 0, t) for t in range(NT)]
    u += [("h", 1, t) for t in range(NT)]
    u += [("m", 0, p) for p in range(KD)]
    u += [("agg", 1, t) for t in range(NT)]
    u += [("mix", 0, t) for t in range(2)]
    u += [("m", 1, p) for p in range(KD)]
    u += [("mix", 0, t) for t in range(2, NT)]
    u += [("mix", 1, t) for t in range(NT)]
    for f, c in GATED:
        u += [("a", f, c), ("b", f, c)]
    u += [("g1", f, c) for c in range(3) for f in range(KH)]
    u += [("g2", f, c) for c in range(3) for f in range(KH)]
    u += [("y", t, h) for t in range(NT) for h in range(2)]
    return {name: i for i, name in enumerate(u)}


UNIT = units()
NBANK = 3
SLAB_END = {KV0 + KD * s + KD - 1: UNIT["kv", s, NT - 1] for s in range(4)}
SLAB_END.update({Q0 + KD - 1: UNIT["q", 3, 2], Q0 + 2 * KD - 1: UNIT["q", 7, 2]})
SLAB_END.update({G0 + KD * (h + 1) - 1: UNIT["h", h, NT - 1] for h in range(2)})
SLAB_END.update({M0 + KD - 1: UNIT["mix", 0, NT - 1], A0 + KD - 1: UNIT["b", 1, 2], B0 + KD - 1: UNIT["b", 3, 2],
                 C0 + KH - 1: UNIT["g1", KH - 1, 2], D0 + KH - 1: UNIT["g2", KH - 1, 2]})


def windows_of(step):
    if 10 <= step < 40:
        return [2 * (step - 10), 2 * (step - 10) + 1]
    if 40 <= step < 60:
        return [20 + step]
    return []


def tile_ended(step):
    return [w // WPT for w in windows_of(step) if w % WPT == WPT - 1]


def build(nc, x, src_cols, dst_cols, dst_rows, wslices, wo, bkv, bq, gb, bo, scales, w3s, out):
    with ExitStack() as ctx:
        def sb(name, shape, dt, where=ctx):
            return where.enter_context(nc.sbuf_tensor(name, shape, dt))

        def sem(name):
            return ctx.enter_context(nc.semaphore(name))

        PS = ctx.enter_context(nc.psum_tensor("PS", [P, 8, 512], F32))
        act_t = sb("act_t", [P, 2, KD, N], F32R)
        ring = sb("ring", [P, RING, 2, 512], F32R)
        stage = sb("stage", [P, STAGE, 512], F32)
        ident = sb("ident", [P, P], F32)
        ones = sb("ones", [P, P], F32)
        st_blk = sb("st_blk", [P, KD, P], F32)
        dinv = sb("dinv", [P, NT], F32)
        deg = sb("deg", [P, 4, NT], F32)
        bq_sb = sb("bq_sb", [P, KD], F32)
        scl = sb("scl", [P, 4, KH], F32)
        stats = sb("stats", [P, 2, 12], F32)
        mv = sb("mv", [P, 2, 2], F32)
        ln = sb("ln", [P, 2, 6], F32)
        cmx = sb("cmx", [P, 16], F32)
        big_i = sb("big_i", [P, 1], I32)
        bounds = sb("bounds", [P, 2 * NWIN], I32)
        wo_sb = sb("wo_sb", [P, 2, 512], F32)
        ph_in = sb("ph_in", [P, 2, N // 2], F32)

        with ExitStack() as r2:
            oh_src = sb("oh_src", [P, 2, STATIC_CHUNKS, P], BF16, r2)
            oh_dst = sb("oh_dst", [P, 2, STATIC_CHUNKS, WCOLS], BF16, r2)
            ex_src = sb("ex_src", [P, EXTRA_CHUNKS, P], BF16, r2)
            ex_dst = sb("ex_dst", [P, EXTRA_CHUNKS, WCOLS], BF16, r2)
            ctile = sb("ctile", [P, 2, P, NT], U16, r2)
            keys = sb("keys", [P, NCH_PAD, 2], F32, r2)
            kcur = sb("kcur", [P, 2, STATIC_CHUNKS, 2], F32, r2)
            kvt = sb("kvt", [P, 2, 512], F32, r2)
            kmin = sb("kmin", [P, 2, 256], F32, r2)
            kexp = sb("kexp", [P, 2, 256], F32, r2)
            phik = sb("phik", [P, 2, 256], F32, r2)
            ksum = sb("ksum", [P, D], F32, r2)
            kvb = sb("kvb", [P, 2, 512], F32, r2)
            iota_c = sb("iota_c", [P, WCOLS], F16, r2)
            ident_u = sb("ident_u", [P, P], U16, r2)
            csum = sb("csum", [P, 2, P], F32, r2)
        with ExitStack() as r2:
            hs = sb("hs", [P, 2, NT, 512], F32R, r2)
        with ExitStack() as r2:
            m1 = sb("m1", [P, 2, KD, 512], F32R, r2)
        hid_t = sb("hid_t", [P, 2, KH, N], F32R)
        sb("pad2", [P, 2 * NT * 512 - 2 * KH * N], F32)
        with ExitStack() as r3:
            xrow = sb("xrow", [P, 2, D], F32, r3)
            xn = sb("xn", [P, 2, D], F32, r3)
            e_src = sb("e_src", [P, NCH_PAD], I32, r3)
            e_dst = sb("e_dst", [P, NCH_PAD], I32, r3)
            e_hi = sb("e_hi", [P, NCH_PAD], I32, r3)
            d_rows = sb("d_rows", [P, ROWS_T, P], I32, r3)
            d_rng = sb("d_rng", [P, 2, ROWS_T], F32, r3)
            d_id = sb("d_id", [P, 2, ROWS_T], F32, r3)
            thr = sb("thr", [P, NWIN], F32, r3)
            score = sb("score", [P, 2, NWIN, ROWS_T], F32, r3)
            smax = sb("smax", [P, 2 * NWIN], F32, r3)
            sall = sb("sall", [P, 2 * NWIN], F32, r3)
            iota_i = sb("iota_i", [P, WCOLS], I32, r3)
        with ExitStack() as r3:
            zblk = sb("zblk", [P, KD, P], F32, r3)
            qmin = sb("qmin", [P, 2, 418], F32, r3)
            qexp = sb("qexp", [P, 2, 418], F32, r3)
            qrel = sb("qrel", [P, 2, 418], F32, r3)
            rec = sb("rec", [P, 2, 418], F32, r3)
            phiq = sb("phiq", [P, 2, N], F32, r3)
        with ExitStack() as r3:
            ctu = sb("ctu", [P, P, NT], U16, r3)
            cf = sb("cf", [P, 2, NT, P], F32R, r3)
            clo = sb("clo", [P, NT, P], F32R, r3)
            xh = sb("xh", [P, 2, 512], F32, r3)
            gt = sb("gt", [P, 512], F32, r3)
            gb_sb = sb("gb_sb", [P, 2, 512], F32, r3)
        xr = sb("xr", [P, 2, D], F32)
        xn2 = sb("xn2", [P, 2, D], F32)
        sil = sb("sil", [P, 2, 418], F32)
        hb = sb("hb", [P, 2, 418], F32)
        w3s_sb = sb("w3s_sb", [P, D], F32)

        phin_d = nc.dram_tensor("phin_d", [KD, P, N], F32, kind="Internal").ap()
        ct_d = nc.dram_tensor("ct_d", [NT, P, P * NT], U16, kind="Internal").ap()
        x1_d = nc.dram_tensor("x1_d", [N, D], F32, kind="Internal").ap()
        x2_d = nc.dram_tensor("x2_d", [N, D], F32, kind="Internal").ap()

        acc_full = sem("acc_full")
        acc_free = [sem(f"acc_free{b}") for b in range(NBANK)]
        stage_in = [sem(f"stage_in{i}") for i in range(STAGE)]
        w_hi = sem("w_hi")
        w_ready = sem("w_ready")
        w_used = sem("w_used")
        consts = sem("consts")
        edges_in = sem("edges_in")
        small_in = sem("small_in")
        x_in = [sem(f"x_in{i}") for i in range(2)]
        kvb_in = [sem(f"kvb_in{i}") for i in range(2)]
        var_ready = sem("var_ready")
        std_ready = sem("std_ready")
        rstd_ready = sem("rstd_ready")
        xn_ready = sem("xn_ready")
        tr_done = sem("tr_done")
        tr_hi = sem("tr_hi")
        tr_lo = sem("tr_lo")
        score_ready = sem("score_ready")
        bounds_max = sem("bounds_max")
        bounds_ready = sem("bounds_ready")
        kmin_ready = sem("kmin_ready")
        kexp_ready = sem("kexp_ready")
        phik_ready = sem("phik_ready")
        ksum_ready = sem("ksum_ready")
        s_done = sem("s_done")
        st_ready = sem("st_ready")
        z_cleared = sem("z_cleared")
        onehot = sem("onehot")
        adj_done = sem("adj_done")
        cnt_ready = sem("cnt_ready")
        ct_ready = sem("ct_ready")
        csum_ready = sem("csum_ready")
        deg_done = sem("deg_done")
        ct_stored = [sem(f"ct_stored{i}") for i in range(2)]
        ex_ready = sem("ex_ready")
        ex_used = sem("ex_used")
        qmin_ready = sem("qmin_ready")
        qact_ready = sem("qact_ready")
        phiq_ready = sem("phiq_ready")
        den_done = sem("den_done")
        den_read = sem("den_read")
        phin_ready = sem("phin_ready")
        phin_stored = [sem(f"phin_stored{i}") for i in range(2)]
        root_deg = sem("root_deg")
        deg_copied = sem("deg_copied")
        dinv_ready = sem("dinv_ready")
        cmx_ready = sem("cmx_ready")
        cmx_all = sem("cmx_all")
        big_ready = sem("big_ready")
        hs_hi = sem("hs_hi")
        hs_lo = sem("hs_lo")
        ctu_in = sem("ctu_in")
        cf_ready = sem("cf_ready")
        clo_ready = sem("clo_ready")
        gb_in = sem("gb_in")
        xh_in = [sem(f"xh_in{i}") for i in range(2)]
        x1_ready = sem("x1_ready")
        x1_stored = [sem(f"x1_stored{i}") for i in range(2)]
        wo_in = [sem(f"wo_in{i}") for i in range(2)]
        m_hi = sem("m_hi")
        ph_loaded = [sem(f"ph_loaded{i}") for i in range(2)]
        ph_hi = sem("ph_hi")
        ph_lo = sem("ph_lo")
        xr_in = [sem(f"xr_in{i}") for i in range(2)]
        x2_stored = [sem(f"x2_stored{i}") for i in range(2)]
        x2h_stored = [sem(f"x2h_stored{i}") for i in range(2)]
        w3s_in = sem("w3s_in")
        hid_hi = sem("hid_hi")
        hid_lo = sem("hid_lo")
        g_hi = sem("g_hi")
        g_lo = sem("g_lo")
        y_in = [sem(f"y_in{i}") for i in range(2)]
        y_ready = sem("y_ready")
        y_stored = [sem(f"y_stored{i}") for i in range(2)]
        dve_chain = sem("dve_chain")
        pool_chain = sem("pool_chain")

        def bank(i):
            return i % NBANK

        def wait_read(eng, i):
            eng.wait_ge(acc_free[bank(i)], i // NBANK + 1)

        def wait_full(eng, i):
            eng.wait_ge(acc_full, i + 1)

        def slice_ready(k):
            return k + 1 if k < M0 else k + 1 - KD

        def wait_released(eng, k):
            if k in SLAB_END:
                wait_full(eng, SLAB_END[k])
            else:
                eng.wait_ge(w_used, k + 1 - sum(e < k for e in SLAB_END))

        def slot(k):
            return k % RING

        def xrows(d, t):
            return d[t * P:t * P + rows(t), :]

        block = ctx.enter_context(nc.Block())

        @block.sync
        def _(sp):
            sp.dma_start(xrow[:, 0, :], xrows(x, 0)).then_inc(x_in[0], 16)
            sp.dma_start(xrow[:, 1, :], xrows(x, 1)).then_inc(x_in[1], 16)
            sp.dma_start(e_src[:], src_cols).then_inc(edges_in, 16)
            sp.dma_start(e_dst[:], dst_cols).then_inc(edges_in, 16)
            sp.dma_start(d_rows[0:ROWS_P], dst_rows).then_inc(edges_in, 16)
            for s in range(2):
                sp.dma_start(kvb[:, s, :], bkv[s:s + 1, :].to_broadcast([P, 512])).then_inc(kvb_in[s], 16)
            sp.dma_start(bq_sb[:], bq).then_inc(small_in, 16)
            sp.dma_start(scl[:], scales).then_inc(small_in, 16)
            for t in range(2, NT):
                sp.wait_ge(xn_ready, t - 1)
                sp.dma_start(xrow[0:rows(t), t % 2, :], xrows(x, t)).then_inc(x_in[t % 2], 16)
            for s in range(2, 4):
                sp.wait_ge(phik_ready, NT * (s - 1))
                sp.dma_start(kvb[:, s % 2, :], bkv[s:s + 1, :].to_broadcast([P, 512])).then_inc(kvb_in[s % 2], 16)

            def phin_store(f):
                sp.wait_ge(phin_ready, 3 * (f + 1))
                sp.dma_start(phin_d[f], phiq[:, f % 2, :]).then_inc(phin_stored[f % 2], 16)

            stored_tiles = 0
            for step in range(64):
                for dt in (tile_ended(step - 2) if step >= 2 else []):
                    sp.wait_ge(ct_ready, dt + 1)
                    sp.dma_start(ct_d[dt], ctile[:, dt % 2].rearrange("p a b -> p (a b)")).then_inc(ct_stored[dt % 2], 16)
                if step >= 40 and (step - 40) % 3 == 2 and (step - 40) // 3 >= 1:
                    phin_store((step - 40) // 3 - 1)
            phin_store(KD - 1)
            for b in range(2):
                sp.wait_ge(phin_stored[b], 16 * KD // 2)
                sp.wait_ge(ct_stored[b], 16 * NT // 2)

            def ctu_load(i):
                if i >= 1:
                    sp.wait_ge(clo_ready, i)
                sp.dma_start(ctu[:].rearrange("p a b -> p (a b)"), ct_d[i % NT]).then_inc(ctu_in, 16)

            def xh_load(i):
                half, t = divmod(i, NT)
                if i >= 2:
                    sp.wait_ge(x1_stored[i % 2], 16 * (i // 2))
                sp.dma_start(xh[0:rows(t), i % 2, :],
                             x[t * P:t * P + rows(t), half * 512:half * 512 + 512]).then_inc(xh_in[i % 2], 16)

            def gb_load(half):
                if half:
                    sp.wait_ge(x1_ready, NT)
                cols = slice(half * 512, half * 512 + 512)
                sp.dma_start(gb_sb[:, 0, :], gb[:, cols].to_broadcast([P, 512])).then_inc(gb_in, 16)
                sp.dma_start(gb_sb[:, 1, :], bo[:, cols].to_broadcast([P, 512])).then_inc(gb_in, 16)

            def wo_load(i):
                half, p = divmod(i, KD)
                if i >= 2:
                    wait_full(sp, UNIT["m", (i - 2) // KD, (i - 2) % KD])
                sp.dma_start(wo_sb[:, i % 2, :], wo[p, :, half * 512:half * 512 + 512]).then_inc(wo_in[i % 2], 16)

            def ph_load(i):
                if i >= 2:
                    sp.wait_ge(ph_lo, i - 1)
                p, h = divmod(i, 2)
                sp.dma_start(ph_in[:, i % 2, :], phin_d[p, :, h * (N // 2):(h + 1) * (N // 2)]).then_inc(ph_loaded[i % 2], 16)

            ctu_load(0)
            gb_load(0)
            xh_load(0)
            xh_load(1)
            for i in range(2 * NT):
                half, t = divmod(i, NT)
                if i == NT:
                    gb_load(1)
                    for p in range(KD):
                        wo_load(p)
                    ph_load(0)
                    ph_load(1)
                if i + 1 < 2 * NT:
                    ctu_load(i + 1)
                if i >= NT:
                    for j in range(2 * (t + 1), min(2 * (t + 1) + 2, 2 * KD)):
                        ph_load(j)
                sp.wait_ge(x1_ready, i + 1)
                sp.dma_start(x1_d[t * P:t * P + rows(t), half * 512:half * 512 + 512],
                             xh[0:rows(t), i % 2, :]).then_inc(x1_stored[i % 2], 16)
                if i + 2 < 2 * NT:
                    xh_load(i + 2)
            for b in range(2):
                sp.wait_ge(x1_stored[b], 16 * NT)
            sp.dma_start(w3s_sb[:], w3s.to_broadcast([P, D])).then_inc(w3s_in, 16)
            wo_load(KD)
            wo_load(KD + 1)

            def xr_load(i):
                half, t = divmod(i, NT)
                if i >= 2:
                    j = i - 2
                    if j < NT:
                        sp.wait_ge(x2h_stored[j % 2], 16 * (j // 2 + 1))
                    else:
                        sp.wait_ge(x2_stored[j % 2], 16 * ((j - NT) // 2 + 1))
                        sp.wait_ge(xn_ready, NT + j - NT + 1)
                if half == 0:
                    sp.dma_start(xr[0:rows(t), i % 2, 0:512], x1_d[t * P:t * P + rows(t), 0:512]).then_inc(xr_in[i % 2], 16)
                else:
                    sp.wait_ge(x2h_stored[t % 2], 16 * (t // 2 + 1))
                    sp.dma_start(xr[0:rows(t), i % 2, 0:512], x2_d[t * P:t * P + rows(t), 0:512]).then_inc(xr_in[i % 2], 16)
                    sp.dma_start(xr[0:rows(t), i % 2, 512:D], x1_d[t * P:t * P + rows(t), 512:D]).then_inc(xr_in[i % 2], 16)

            xr_load(0)
            xr_load(1)
            for i in range(2 * NT):
                half, t = divmod(i, NT)
                if i == 2:
                    for p in range(2, KD):
                        wo_load(KD + p)
                wait_read(sp, UNIT["mix", half, t])
                cols = slice(half * 512, half * 512 + 512)
                sp.dma_start(x2_d[t * P:t * P + rows(t), cols], xr[0:rows(t), i % 2, cols]).then_inc(
                    (x2_stored if half else x2h_stored)[i % 2], 16)
                if i + 2 < 2 * NT:
                    xr_load(i + 2)

            def y_load(t):
                if t >= 2:
                    sp.wait_ge(y_stored[t % 2], 16 * (t // 2))
                sp.dma_start(xr[0:rows(t), t % 2, :], xrows(x2_d, t)).then_inc(y_in[t % 2], 16)

            for b in range(2):
                sp.wait_ge(x2_stored[b], 16 * NT // 2)
            sp.wait_ge(xn_ready, 2 * NT)
            y_load(0)
            y_load(1)
            for t in range(NT):
                sp.wait_ge(y_ready, 2 * t + 2)
                sp.dma_start(xrows(out, t), xr[0:rows(t), t % 2, :]).then_inc(y_stored[t % 2], 16)
                if t + 2 < NT:
                    y_load(t + 2)
            for b in range(2):
                sp.wait_ge(y_stored[b], 16 * NT // 2)

        @block.gpsimd
        def _(pool):
            chain = [0]

            def link(ins):
                chain[0] += 1
                ins.then_inc(pool_chain, 1)
                pool.wait_ge(pool_chain, chain[0])

            slices = list(range(M0)) + list(range(A0, NSLICE))

            def load(n):
                pool.dma_start(stage[:, n % STAGE, :], wslices[n]).then_inc(stage_in[n % STAGE], 16)

            for n in range(STAGE):
                load(n)
            link(nc.gpsimd.memset(ident[:], 0.0))
            nc.gpsimd.affine_select(out=ident[:], in_=ident[:], compare_op=ALU.not_equal, fill=1.0, base=0,
                                    pattern=[[-1, P]], channel_multiplier=1).then_inc(consts, 1)

            def split(n):
                k = slices[n]
                pool.wait_ge(stage_in[n % STAGE], 16 * (n // STAGE + 1))
                if k >= RING:
                    wait_released(pool, k - RING)
                nc.gpsimd.tensor_copy(ring[:, slot(k), 0, :], stage[:, n % STAGE, :]).then_inc(w_hi, 1)
                pool.wait_ge(w_hi, n + 1)
                nc.gpsimd.tensor_tensor(ring[:, slot(k), 1, :], stage[:, n % STAGE, :],
                                        ring[:, slot(k), 0, :].bitcast(F32), ALU.subtract).then_inc(w_ready, 1)
                if n + STAGE < len(slices):
                    pool.wait_ge(w_ready, n + 1)
                    load(n + STAGE)

            for n in range(8):
                split(n)
            nc.gpsimd.memset(ones[:], 1.0).then_inc(consts, 1)
            nc.gpsimd.memset(st_blk[:], 0.0).then_inc(consts, 1)
            nc.gpsimd.iota(iota_i[:], [[1, WCOLS]], base=0, channel_multiplier=0).then_inc(consts, 1)
            nc.gpsimd.iota(d_id[:, 0, :], [[1, ROWS_T]], base=1, channel_multiplier=ROWS_T,
                           allow_small_or_imprecise_dtypes=True).then_inc(consts, 1)
            nc.gpsimd.iota(d_id[:, 1, :], [[-1, ROWS_T]], base=int(BIG), channel_multiplier=-ROWS_T,
                           allow_small_or_imprecise_dtypes=True).then_inc(consts, 1)
            nc.gpsimd.iota(thr[:], [[WIN, NWIN]], base=0, channel_multiplier=0,
                           allow_small_or_imprecise_dtypes=True).then_inc(consts, 1)
            pool.wait_ge(score_ready, 1)
            nc.gpsimd.partition_all_reduce(sall[:], smax[:], P, RMAX).then_inc(bounds_max, 1)
            for n in range(8, 58):
                split(n)
            pool.wait_ge(cmx_ready, 1)
            nc.gpsimd.partition_all_reduce(cmx[:, 12:13], cmx[:, 11:12], P, RMAX).then_inc(cmx_all, 1)
            for n in range(58, len(slices)):
                split(n)

        @block.scalar
        def _(act):
            def ln_root(i):
                act.wait_ge(var_ready, i + 1)
                nc.scalar.activation(ln[0:rows(i % NT), i % 2, 1:2], ln[0:rows(i % NT), i % 2, 0:1],
                                     ACT.Sqrt).then_inc(std_ready, 1)

            def ln_apply(i):
                t = i % NT
                r = rows(t)
                act.wait_ge(rstd_ready, i + 1)
                if i >= 2:
                    act.wait_ge(tr_done, 2 * (i - 1))
                if i < NT:
                    to, of = xn[0:r, i % 2, :], xrow[0:r, i % 2, :]
                else:
                    to, of = xn2[0:r, i % 2, :], xr[0:r, i % 2, :]
                nc.scalar.activation(to, of, ACT.Identity, bias=ln[0:r, i % 2, 5:6],
                                     scale=ln[0:r, i % 2, 4:5]).then_inc(xn_ready, 1)

            def transposed_hi(i):
                t = i % NT
                for g in range(2):
                    act.wait_ge(tr_done, 2 * i + g + 1)
                    nc.scalar.activation(
                        act_t[:, 0, 4 * g:4 * g + 4, t * P:t * P + rows(t)],
                        PS[:, 5 + g, :].rearrange("p (a b) -> p a b", a=4)[:, :, 0:rows(t)],
                        ACT.Copy).then_inc(tr_hi, 1)

            def adj_out(w):
                dt, j = divmod(w, WPT)
                act.wait_ge(adj_done, w + 1)
                if j == 0 and dt >= 2:
                    act.wait_ge(ct_stored[dt % 2], 16 * (dt // 2))
                    act.wait_ge(csum_ready, dt - 1)
                nc.scalar.activation(
                    ctile[:, dt % 2, j * WIN:(j + 1) * WIN, :],
                    PS[:, 5 + w % 2, 0:WCOLS].rearrange("p (a b) -> p a b", a=WIN),
                    ACT.Copy).then_inc(cnt_ready, 1)

            for i in range(2):
                ln_root(i)
                ln_apply(i)
            transposed_hi(0)
            for step in range(40):
                r = rows(step % NT)
                if step < 8:
                    ln_root(step + 2)
                    ln_apply(step + 2)
                if step < 9:
                    transposed_hi(step + 1)
                act.wait_ge(kmin_ready, step + 1)
                nc.scalar.activation(kexp[0:r, step % 2, :], kmin[0:r, step % 2, :], ACT.Exp).then_inc(kexp_ready, 1)
                for w in (windows_of(step - 1) if step else []):
                    adj_out(w)
            act.wait_ge(s_done, 40)
            act.wait_ge(consts, 3)
            s_ps = PS[:, 3:5, :].rearrange("p a (b c) -> p (a b) c", c=P)
            for g in range(2):
                o = slice(64 * g, 64 * g + 64)
                nc.scalar.activation(st_blk[o, :, o], s_ps[o, :, o], ACT.Copy).then_inc(st_ready, 1)
            for i in range(2):
                u = UNIT["z", i]
                wait_full(act, u)
                act.wait_ge(z_cleared, 1)
                z_ps = PS[:, bank(u), :].rearrange("p (a b) -> p a b", a=4)
                nc.scalar.activation(zblk[0:64, 4 * i:4 * i + 4, 0:64], z_ps[0:64, :, 0:64], ACT.Copy)
                nc.scalar.activation(zblk[64:P, 4 * i:4 * i + 4, 64:P], z_ps[64:P, :, 64:P],
                                     ACT.Copy).then_inc(acc_free[bank(u)], 1)
            act.wait_ge(small_in, 32)
            for i in range(24):
                f, c = divmod(i, 3)
                n = CHUNKS[c][1]
                u = UNIT["q", f, c]
                act.wait_ge(qmin_ready, i + 1)
                if i >= 2:
                    act.wait_ge(phiq_ready, i - 1)
                nc.scalar.activation(qexp[:, i % 2, 0:n], qmin[:, i % 2, 0:n], ACT.Exp).then_inc(qact_ready, 1)
                nc.scalar.activation(qrel[:, i % 2, 0:n], PS[:, bank(u), 0:n], ACT.Relu,
                                     bias=bq_sb[:, f:f + 1]).then_inc(acc_free[bank(u)], 1)
                for w in windows_of(40 + i - 1):
                    adj_out(w)

            def h_out(half, t):
                u = UNIT["h", half, t]
                wait_full(act, u)
                if half:
                    wait_full(act, UNIT["agg", 0, NT - 1])
                nc.scalar.activation(hs[0:rows(t), 0, t, :], PS[0:rows(t), bank(u), :], ACT.Copy,
                                     scale=dinv[0:rows(t), t:t + 1]).then_inc(hs_hi, 1)

            def cf_out(i):
                act.wait_ge(ctu_in, 16 * (i + 1))
                if i >= 2:
                    wait_full(act, UNIT["agg", (i - 2) // NT, (i - 2) % NT])
                nc.scalar.activation(cf[:, i % 2], ctu[:].rearrange("p a b -> p b a"), ACT.Copy).then_inc(cf_ready, 1)

            act.wait_ge(deg_copied, 1)
            nc.scalar.activation(deg[:, 1, :], deg[:, 0, :], ACT.Sqrt).then_inc(root_deg, 1)
            act.wait_ge(dinv_ready, 1)
            for b in range(2):
                act.wait_ge(ct_stored[b], 16 * NT // 2)
            for t in range(NT):
                h_out(0, t)
            cf_out(0)
            for t in range(NT):
                cf_out(t + 1)
            for t in range(NT):
                h_out(1, t)

            def m_out(half, p):
                u = UNIT["m", half, p]
                wait_full(act, u)
                to = m1[:, 0, p, :] if half else ring[:, slot(M0 + p), 0, :]
                nc.scalar.activation(to, PS[:, bank(u), :], ACT.Copy).then_inc(m_hi, 1)

            wait_full(act, UNIT["h", 1, NT - 1])
            for p in range(KD):
                m_out(0, p)

            def ph_split(i):
                p, h = divmod(i, 2)
                act.wait_ge(ph_loaded[i % 2], 16 * (i // 2 + 1))
                o = slice(h * (N // 2), (h + 1) * (N // 2))
                nc.scalar.activation(act_t[:, 0, p, o], ph_in[:, i % 2, :], ACT.Copy).then_inc(ph_hi, 1)

            for t in range(NT):
                if t + 1 < NT:
                    cf_out(NT + t + 1)
                for i in range(2 * t, min(2 * t + 2, 2 * KD)):
                    ph_split(i)
            wait_full(act, UNIT["agg", 1, NT - 1])
            for p in range(KD):
                m_out(1, p)
            for t in range(NT + 2):
                if t < NT:
                    ln_root(NT + t)
                    ln_apply(NT + t)
                if t >= 1 and t - 1 < NT:
                    transposed_hi(NT + t - 1)
            for i, (f, c) in enumerate(GATED):
                o, n = CHUNKS[c]
                u = UNIT["a", f, c]
                wait_full(act, u)
                if i >= 2:
                    wait_read(act, UNIT["b", *GATED[i - 2]])
                nc.scalar.activation(sil[:, i % 2, 0:n], PS[:, bank(u), 0:n], ACT.Silu,
                                     scale=scl[:, 0, f:f + 1]).then_inc(acc_free[bank(u)], 1)
                wait_read(act, UNIT["b", f, c])
                nc.scalar.activation(hid_t[:, 0, f, o:o + n], hb[:, i % 2, 0:n], ACT.Copy).then_inc(hid_hi, 1)
            for g in range(2):
                for i in range(12):
                    c, f = divmod(i, KH)
                    o, n = CHUNKS[c]
                    u = UNIT[("g1", "g2")[g], f, c]
                    j = 12 * g + i
                    wait_full(act, u)
                    if j == 0:
                        act.wait_ge(hid_lo, 12)
                    if j >= 2:
                        act.wait_ge(g_lo, j - 1)
                    nc.scalar.activation(hb[:, i % 2, 0:n], PS[:, bank(u), 0:n], ACT.Gelu,
                                         scale=scl[:, 2 + g, f:f + 1]).then_inc(acc_free[bank(u)], 1)
                    wait_read(act, u)
                    to = hid_t if g else act_t
                    nc.scalar.activation(to[:, 0, f, o:o + n], hb[:, i % 2, 0:n], ACT.Copy).then_inc(g_hi, 1)

        @block.vector
        def _(dve):
            chain = [0]

            def link(ins):
                chain[0] += 1
                ins.then_inc(dve_chain, 1)
                dve.wait_ge(dve_chain, chain[0])

            def ln_stats(i):
                t = i % NT
                r = rows(t)
                src = (xrow if i < NT else xr)[0:r, i % 2, :]
                for g in range(2):
                    link(dve.bn_stats(stats[0:r, i % 2, 6 * g:6 * g + 6], src[:, 512 * g:512 * g + 512]))
                link(dve.bn_aggr(mv[0:r, i % 2, :], stats[0:r, i % 2, :]))
                dve.tensor_scalar(ln[0:r, i % 2, 0:1], mv[0:r, i % 2, 1:2], LN_EPS, None,
                                  ALU.add).then_inc(var_ready, 1)

            def newton(v, root, y, tmp, tmp2, last):
                link(dve.reciprocal(y, root))
                link(dve.tensor_tensor(tmp, y, y, ALU.mult))
                link(dve.tensor_tensor(tmp2, tmp, v, ALU.mult))
                link(dve.tensor_scalar(tmp, tmp2, -0.5, 1.5, ALU.mult, ALU.add))
                return dve.tensor_tensor(last, y, tmp, ALU.mult)

            def ln_finish(i):
                r = rows(i % NT)
                c = [ln[0:r, i % 2, j:j + 1] for j in range(6)]
                dve.wait_ge(std_ready, i + 1)
                dve.wait_ge(var_ready, i + 1)
                link(newton(c[0], c[1], c[2], c[3], c[5], c[4]))
                dve.scalar_tensor_tensor(c[5], mv[0:r, i % 2, 0:1], -1.0, c[4], ALU.mult, ALU.mult).then_inc(rstd_ready, 1)

            def transposed_lo(i):
                t = i % NT
                for g in range(2):
                    dve.wait_ge(tr_hi, 2 * i + g + 1)
                    o = slice(t * P, t * P + rows(t))
                    dve.tensor_tensor(act_t[:, 1, 4 * g:4 * g + 4, o],
                                      PS[:, 5 + g, :].rearrange("p (a b) -> p a b", a=4)[:, :, 0:rows(t)],
                                      act_t[:, 0, 4 * g:4 * g + 4, o].bitcast(F32), ALU.subtract).then_inc(tr_lo, 1)

            def edge_list():
                dve.wait_ge(edges_in, 48)
                dve.wait_ge(consts, 7)
                link(dve.tensor_scalar(e_hi[:], e_src[:], 7, None, ALU.logical_shift_right))
                link(dve.tensor_scalar(e_src[:], e_src[:], P - 1, None, ALU.bitwise_and))
                link(dve.tensor_copy(keys[:, :, 0], e_src[:]))
                link(dve.scalar_tensor_tensor(keys[:, :, 1], e_dst[:], float(NT), e_hi[:], ALU.mult, ALU.add))
                link(dve.tensor_copy(iota_c[:], iota_i[:]))
                link(dve.tensor_copy(ident_u[:], ident[:]))
                link(dve.memset(smax[:], 0.0))
                a = slice(0, ROWS_P)
                link(dve.tensor_reduce(d_rng[a, 0, :], d_rows[a], AX.X, ALU.min))
                link(dve.tensor_reduce(d_rng[a, 1, :], d_rows[a], AX.X, ALU.max))
                link(dve.tensor_scalar(d_rng[a, 0, :], d_rng[a, 0, :], 1.0 - WIN, None, ALU.add))
                for t in range(ROWS_T):
                    lo, hi = score[a, 0, :, t], score[a, 1, :, t]
                    link(dve.tensor_scalar(lo, thr[a], d_rng[a, 0, t:t + 1], None, ALU.is_ge))
                    link(dve.scalar_tensor_tensor(lo, thr[a], d_rng[a, 1, t:t + 1], lo, ALU.is_le, ALU.mult))
                    link(dve.tensor_scalar(hi, lo, d_id[a, 0, t:t + 1], None, ALU.mult))
                    link(dve.tensor_scalar(lo, lo, d_id[a, 1, t:t + 1], None, ALU.mult))
                dve.tensor_reduce(smax[a].rearrange("p (a b) -> p a b", a=2), score[a], AX.X, ALU.max).then_inc(score_ready, 1)

            def edge_bounds():
                dve.wait_ge(bounds_max, 1)
                link(dve.tensor_scalar(smax[:, 0:NWIN], sall[:, 0:NWIN], -1.0, BIG, ALU.mult, ALU.add))
                link(dve.tensor_scalar(smax[:, 0:NWIN], smax[:, 0:NWIN], float(NCH), None, ALU.min))
                link(dve.tensor_copy(bounds[:, 0:NWIN], smax[:, 0:NWIN]))
                dve.tensor_copy(bounds[:, NWIN:], sall[:, NWIN:]).then_inc(bounds_ready, 1)

            def first_chunk(w):
                return dve.value_load(bounds[0:1, w:w + 1], min_val=0, max_val=NCH)

            def end_chunk(w):
                return dve.value_load(bounds[0:1, NWIN + w:NWIN + w + 1], min_val=0, max_val=NCH + 1)

            trips = dve.alloc_register("extra_trips")
            dve.reg_mov(trips, 0)

            def window(w):
                first = first_chunk(w)
                end = end_chunk(w)
                b = w % 2
                if w >= 2:
                    dve.wait_ge(adj_done, w - 1)
                link(dve.tensor_copy(kcur[:, b], keys[:, bass.ds(first, STATIC_CHUNKS), :]))
                for j in range(STATIC_CHUNKS):
                    dve.tensor_scalar(oh_src[:, b, j, :], iota_c[:, 0:P], kcur[:, b, j, 0:1], None, ALU.is_equal)
                    ins = dve.tensor_scalar(oh_dst[:, b, j, :], iota_c[:], kcur[:, b, j, 1:2], float(-WCOLS * w),
                                            ALU.subtract, ALU.is_equal)
                ins.then_inc(onehot, 1)
                with dve.If(end > first + STATIC_CHUNKS):
                    with dve.Fori(first + STATIC_CHUNKS, end, EXTRA_CHUNKS) as c:
                        for j in range(EXTRA_CHUNKS):
                            at = bass.ds(c + j, 1)
                            dve.tensor_scalar(ex_src[:, j, :], iota_c[:, 0:P], keys[:, at, 0], None, ALU.is_equal)
                            ins = dve.tensor_scalar(ex_dst[:, j, :], iota_c[:], keys[:, at, 1], float(-WCOLS * w),
                                                    ALU.subtract, ALU.is_equal)
                        ins.then_inc(ex_ready, 1)
                        dve.reg_add(trips, trips, 1)
                        dve.wait_ge(ex_used, dve.snap(trips))

            def count_tile(dt):
                dve.wait_ge(cnt_ready, WPT * (dt + 1))
                c = ctile[:, dt % 2, :, dt]
                dve.tensor_tensor(c, c, ident_u[:], ALU.add).then_inc(ct_ready, 1)
                dve.wait_ge(ct_ready, dt + 1)
                if dt >= 2:
                    dve.wait_ge(deg_done, dt - 1)
                dve.tensor_reduce(csum[:, dt % 2, :], ctile[:, dt % 2], AX.X, ALU.add).then_inc(csum_ready, 1)
                dve.wait_ge(csum_ready, dt + 1)
                link(dve.tensor_reduce(cmx[:, dt:dt + 1], csum[:, dt % 2, :], AX.X, ALU.max))

            for i in range(2):
                dve.wait_ge(x_in[i % 2], 16)
                ln_stats(i)
                ln_finish(i)
            edge_list_at = 2
            transposed_lo(0)
            for step in range(40):
                s, t = divmod(step, NT)
                r = rows(t)
                b = step % 2
                if step < 8:
                    dve.wait_ge(x_in[step % 2], 16 * ((step + 2) // 2 + 1))
                    ln_stats(step + 2)
                    ln_finish(step + 2)
                if step < 9:
                    transposed_lo(step + 1)
                if step == edge_list_at:
                    edge_list()
                if step == 8:
                    edge_bounds()
                u = UNIT["kv", s, t]
                wait_full(dve, u)
                dve.wait_ge(kvb_in[s % 2], 16 * (s // 2 + 1))
                if step >= 2:
                    dve.wait_ge(s_done, step - 1)
                dve.tensor_tensor(kvt[0:r, b, :], PS[0:r, bank(u), :], kvb[0:r, s % 2, :], ALU.add).then_inc(acc_free[bank(u)], 1)
                wait_read(dve, u)
                dve.tensor_scalar(kmin[0:r, b, :], kvt[0:r, b, 0:256], 0.0, None, ALU.min).then_inc(kmin_ready, 1)
                dve.wait_ge(kexp_ready, step + 1)
                dve.scalar_tensor_tensor(phik[0:r, b, :], kvt[0:r, b, 0:256], 0.0, kexp[0:r, b, :],
                                         ALU.max, ALU.add).then_inc(phik_ready, 1)
                dve.wait_ge(phik_ready, step + 1)
                z = ksum[0:r, 256 * s:256 * s + 256]
                if t == 0:
                    dve.tensor_copy(z, phik[0:r, b, :]).then_inc(ksum_ready, 1)
                else:
                    dve.tensor_tensor(z, z, phik[0:r, b, :], ALU.add).then_inc(ksum_ready, 1)
                if step == 10:
                    dve.wait_ge(bounds_ready, 1)
                for w in windows_of(step):
                    window(w)
                for dt in (tile_ended(step - 2) if step >= 2 else []):
                    count_tile(dt)
                dve.wait_ge(ksum_ready, step + 1)
            wait_full(dve, UNIT["z", 0])
            dve.memset(zblk[:], 0.0).then_inc(z_cleared, 1)
            dve.wait_ge(small_in, 32)

            def q_out(i):
                f, c = divmod(i, 3)
                o, n = CHUNKS[c]
                u = UNIT["q", f, c]
                wait_full(dve, u)
                dve.tensor_scalar(qmin[:, i % 2, 0:n], PS[:, bank(u), 0:n], bq_sb[:, f:f + 1], 0.0,
                                  ALU.add, ALU.min).then_inc(qmin_ready, 1)
                dve.wait_ge(qact_ready, i + 1)
                wait_read(dve, u)
                if f >= 2 and c == 0:
                    dve.wait_ge(phin_stored[f % 2], 16 * (f // 2))
                dve.tensor_tensor(phiq[:, f % 2, o:o + n], qexp[:, i % 2, 0:n], qrel[:, i % 2, 0:n],
                                  ALU.add).then_inc(phiq_ready, 1)

            def den_out(i):
                f, c = divmod(i, 3)
                o, n = CHUNKS[c]
                dve.wait_ge(den_done, i + 1)
                dve.tensor_scalar(rec[:, i % 2, 0:n], PS[:, 3 + i % 2, 0:n], DEN_EPS, None, ALU.add).then_inc(den_read, 1)
                dve.wait_ge(den_read, i + 1)
                link(dve.reciprocal(rec[:, i % 2, 0:n], rec[:, i % 2, 0:n]))
                dve.tensor_tensor(phiq[:, f % 2, o:o + n], phiq[:, f % 2, o:o + n], rec[:, i % 2, 0:n],
                                  ALU.mult).then_inc(phin_ready, 1)

            for i in range(24):
                q_out(i)
                if i >= 3:
                    den_out(i - 3)
                for w in windows_of(40 + i):
                    window(w)
                for dt in tile_ended(40 + i - 2):
                    count_tile(dt)
            link(dve.tensor_reduce(cmx[:, 11:12], cmx[:, 0:NT], AX.X, ALU.max))
            dve.tensor_copy(cmx[:, 13:14], cmx[:, 11:12]).then_inc(cmx_ready, 1)
            link(dve.memset(deg[:], 1.0))
            dve.wait_ge(deg_done, NT)
            last = rows(NT - 1)
            link(dve.tensor_copy(deg[:, 0, 0:NT - 1], PS[:, 7, 0:NT - 1]))
            dve.tensor_copy(deg[0:last, 0, NT - 1:NT], PS[0:last, 7, NT - 1:NT]).then_inc(deg_copied, 1)
            dve.wait_ge(root_deg, 1)
            newton(deg[:, 0, :], deg[:, 1, :], deg[:, 2, :], deg[:, 3, :], deg[:, 1, :], dinv[:]).then_inc(dinv_ready, 1)
            dve.wait_ge(dinv_ready, 1)
            dve.wait_ge(cmx_all, 1)
            dve.tensor_copy(big_i[:], cmx[:, 12:13]).then_inc(big_ready, 1)

            def h_lo(half, t):
                r = rows(t)
                u = UNIT["h", half, t]
                dve.wait_ge(hs_hi, NT * half + t + 1)
                dve.scalar_tensor_tensor(hs[0:r, 1, t, :], PS[0:r, bank(u), :], dinv[0:r, t:t + 1],
                                         hs[0:r, 0, t, :].bitcast(F32), ALU.mult, ALU.subtract).then_inc(acc_free[bank(u)], 1)

            def c_lo(i):
                dve.wait_ge(cf_ready, i + 1)
                if i >= 1:
                    wait_full(dve, UNIT["agg", (i - 1) // NT, (i - 1) % NT])
                dve.tensor_tensor(clo[:], ctu[:].rearrange("p a b -> p b a"), cf[:, i % 2].bitcast(F32),
                                  ALU.subtract).then_inc(clo_ready, 1)

            def agg_out(i):
                half, t = divmod(i, NT)
                r = rows(t)
                u = UNIT["agg", half, t]
                wait_full(dve, u)
                dve.wait_ge(gb_in, 32 * (half + 1))
                dve.wait_ge(xh_in[i % 2], 16 * (i // 2 + 1))
                a = xh[0:r, i % 2, :]
                dve.scalar_tensor_tensor(gt[0:r, :], PS[0:r, bank(u), :], dinv[0:r, t:t + 1], gb_sb[0:r, 0, :],
                                         ALU.mult, ALU.add).then_inc(acc_free[bank(u)], 1)
                wait_read(dve, u)
                link(dve.scalar_tensor_tensor(a, gt[0:r, :], 0.0, a, ALU.max, ALU.add))
                dve.tensor_tensor(a, a, gb_sb[0:r, 1, :], ALU.add).then_inc(x1_ready, 1)

            for t in range(NT):
                h_lo(0, t)
                if t < 3:
                    den_out(21 + t)
            c_lo(0)
            for t in range(NT):
                agg_out(t)
                c_lo(t + 1)
            for t in range(NT):
                h_lo(1, t)

            def m_lo(half, p):
                u = UNIT["m", half, p]
                dve.wait_ge(m_hi, KD * half + p + 1)
                if half:
                    to, hi = m1[:, 1, p, :], m1[:, 0, p, :]
                else:
                    to, hi = ring[:, slot(M0 + p), 1, :], ring[:, slot(M0 + p), 0, :]
                dve.tensor_tensor(to, PS[:, bank(u), :], hi.bitcast(F32), ALU.subtract).then_inc(acc_free[bank(u)], 1)

            for p in range(KD):
                m_lo(0, p)
            for t in range(NT):
                for i in range(2 * t, min(2 * t + 2, 2 * KD)):
                    p, h = divmod(i, 2)
                    o = slice(h * (N // 2), (h + 1) * (N // 2))
                    dve.wait_ge(ph_hi, i + 1)
                    dve.tensor_tensor(act_t[:, 1, p, o], ph_in[:, i % 2, :], act_t[:, 0, p, o].bitcast(F32),
                                      ALU.subtract).then_inc(ph_lo, 1)
                agg_out(NT + t)
                if t + 1 < NT:
                    c_lo(NT + t + 1)

            def mix_out(i):
                half, t = divmod(i, NT)
                r = rows(t)
                u = UNIT["mix", half, t]
                wait_full(dve, u)
                if half:
                    dve.wait_ge(xr_in[i % 2], 16 * (NT // 2) + 32 * ((i - NT) // 2 + 1))
                else:
                    dve.wait_ge(xr_in[i % 2], 16 * (i // 2 + 1))
                a = xr[0:r, i % 2, 512 * half:512 * half + 512]
                dve.tensor_tensor(a, PS[0:r, bank(u), :], a, ALU.add).then_inc(acc_free[bank(u)], 1)
                wait_read(dve, u)

            for t in range(NT):
                if t == 2:
                    for p in range(KD):
                        m_lo(1, p)
                mix_out(t)
            for t in range(NT + 1):
                if t < NT:
                    mix_out(NT + t)
                    ln_stats(NT + t)
                    ln_finish(NT + t)
                if t >= 1:
                    transposed_lo(NT + t - 1)
            for i, (f, c) in enumerate(GATED):
                o, n = CHUNKS[c]
                ua, ub = UNIT["a", f, c], UNIT["b", f, c]
                wait_read(dve, ua)
                wait_full(dve, ub)
                dve.scalar_tensor_tensor(hb[:, i % 2, 0:n], PS[:, bank(ub), 0:n], scl[:, 1, f:f + 1],
                                         sil[:, i % 2, 0:n], ALU.mult, ALU.mult).then_inc(acc_free[bank(ub)], 1)
                dve.wait_ge(hid_hi, i + 1)
                dve.tensor_tensor(hid_t[:, 1, f, o:o + n], hb[:, i % 2, 0:n], hid_t[:, 0, f, o:o + n].bitcast(F32),
                                  ALU.subtract).then_inc(hid_lo, 1)
            for j in range(24):
                g, i = divmod(j, 12)
                c, f = divmod(i, KH)
                o, n = CHUNKS[c]
                u = UNIT[("g1", "g2")[g], f, c]
                to = hid_t if g else act_t
                dve.wait_ge(g_hi, j + 1)
                dve.tensor_tensor(to[:, 1, f, o:o + n], hb[:, i % 2, 0:n], to[:, 0, f, o:o + n].bitcast(F32),
                                  ALU.subtract).then_inc(g_lo, 1)
            dve.wait_ge(w3s_in, 16)
            for t in range(NT):
                r = rows(t)
                dve.wait_ge(y_in[t % 2], 16 * (t // 2 + 1))
                for h in range(2):
                    u = UNIT["y", t, h]
                    wait_full(dve, u)
                    o = slice(512 * h, 512 * h + 512)
                    dve.tensor_tensor(xn2[0:r, h, 0:512], PS[0:r, bank(u), :], w3s_sb[0:r, o], ALU.mult).then_inc(acc_free[bank(u)], 1)
                    wait_read(dve, u)
                    dve.tensor_tensor(xr[0:r, t % 2, o], xr[0:r, t % 2, o], xn2[0:r, h, 0:512], ALU.add).then_inc(y_ready, 1)

        @block.tensor
        def _(pe):
            def open_unit(u):
                if u >= NBANK:
                    pe.wait_ge(acc_free[bank(u)], u // NBANK)
                return bank(u)

            def transpose_tile(i):
                t = i % NT
                r = rows(t)
                src = xn if i < NT else xn2
                pe.wait_ge(xn_ready, i + 1)
                if i >= 1:
                    pe.wait_ge(tr_lo, 2 * i)
                for g in range(2):
                    for j in range(4):
                        e = 4 * g + j
                        ins = pe.transpose(PS[:, 5 + g, j * P:j * P + r], src[0:r, i % 2, e * P:(e + 1) * P],
                                           ident[0:r, 0:r])
                    ins.then_inc(tr_done, 1)

            def node_rows(hl, k, t):
                return act_t[:, hl, k, t * P:t * P + rows(t)]

            def gemm_rows(u, t, k0, first, last):
                b = open_unit(u)
                out_ap = PS[0:rows(t), b, :]
                for k in range(KD):
                    if first:
                        pe.wait_ge(w_ready, slice_ready(k0 + k))
                    pe.matmul(out_ap, node_rows(0, k, t), ring[:, slot(k0 + k), 0, :], start=(k == 0), stop=False)
                    pe.matmul(out_ap, node_rows(1, k, t), ring[:, slot(k0 + k), 0, :], start=False, stop=False)
                    ins = pe.matmul(out_ap, node_rows(0, k, t), ring[:, slot(k0 + k), 1, :], start=False, stop=(k == KD - 1))
                    if last and k < KD - 1:
                        ins.then_inc(w_used, 1)
                ins.then_inc(acc_full, 1)

            def kv_sum(step):
                s, t = divmod(step, NT)
                r = rows(t)
                pe.wait_ge(phik_ready, step + 1)
                for p in range(2):
                    o = 256 * (s % 2) + P * p
                    ins = pe.matmul(PS[:, 3 + s // 2, o:o + P], kvt[0:r, step % 2, 256 + P * p:256 + P * (p + 1)],
                                    phik[0:r, step % 2, P * p:P * (p + 1)], start=(t == 0 and p == 0),
                                    stop=(t == NT - 1), skip_group_check=True)
                ins.then_inc(s_done, 1)

            trips = pe.alloc_register("extra_trips_pe")
            pe.reg_mov(trips, 0)

            def window(w):
                b = 5 + w % 2
                first = pe.value_load(bounds[0:1, w:w + 1], min_val=0, max_val=NCH)
                end = pe.value_load(bounds[0:1, NWIN + w:NWIN + w + 1], min_val=0, max_val=NCH + 1)
                pe.wait_ge(onehot, w + 1)
                if w >= 2:
                    pe.wait_ge(cnt_ready, w - 1)
                for j in range(STATIC_CHUNKS - 1):
                    pe.matmul(PS[:, b, 0:WCOLS], oh_src[:, w % 2, j, :], oh_dst[:, w % 2, j, :],
                              start=(j == 0), stop=False)
                with pe.If(end > first + STATIC_CHUNKS):
                    with pe.Fori(first + STATIC_CHUNKS, end, EXTRA_CHUNKS):
                        pe.reg_add(trips, trips, 1)
                        pe.wait_ge(ex_ready, pe.snap(trips))
                        for j in range(EXTRA_CHUNKS):
                            ins = pe.matmul(PS[:, b, 0:WCOLS], ex_src[:, j, :], ex_dst[:, j, :],
                                            start=False, stop=False)
                        ins.then_inc(ex_used, 1)
                j = STATIC_CHUNKS - 1
                pe.matmul(PS[:, b, 0:WCOLS], oh_src[:, w % 2, j, :], oh_dst[:, w % 2, j, :],
                          start=False, stop=True).then_inc(adj_done, 1)

            def degree(dt):
                pe.wait_ge(csum_ready, dt + 1)
                pe.matmul(PS[0:rows(dt), 7, dt:dt + 1], csum[:, dt % 2, 0:rows(dt)], ones[:, 0:1],
                          start=True, stop=True).then_inc(deg_done, 1)

            def around(step):
                for w in (windows_of(step - 1) if step >= 1 else []):
                    window(w)
                for dt in (tile_ended(step - 3) if step >= 3 else []):
                    degree(dt)

            pe.wait_ge(consts, 1)
            transpose_tile(0)
            for step in range(40):
                s, t = divmod(step, NT)
                if step < 9:
                    transpose_tile(step + 1)
                if step == 10:
                    pe.wait_ge(bounds_ready, 1)
                if s == 0:
                    pe.wait_ge(tr_lo, 2 * (t + 1))
                gemm_rows(UNIT["kv", s, t], t, KV0 + KD * s, t == 0, t == NT - 1)
                if step >= 1:
                    kv_sum(step - 1)
                around(step)
            kv_sum(39)
            pe.wait_ge(consts, 2)
            pe.wait_ge(ksum_ready, 40)
            for i in range(2):
                u = UNIT["z", i]
                b = open_unit(u)
                for j in range(4):
                    ins = pe.matmul(PS[:, b, P * j:P * (j + 1)], ksum[:, P * (4 * i + j):P * (4 * i + j + 1)], ones[:],
                                    start=True, stop=True)
                ins.then_inc(acc_full, 1)

            def gemm_cols(u, f, c, k0, nk, x_t, first, last):
                o, n = CHUNKS[c]
                b = open_unit(u)
                out_ap = PS[:, b, 0:n]
                for k in range(nk):
                    if first:
                        pe.wait_ge(w_ready, slice_ready(k0 + k))
                    w = [ring[:, slot(k0 + k), hl, f * P:(f + 1) * P] for hl in range(2)]
                    pe.matmul(out_ap, w[0], x_t[:, 0, k, o:o + n], start=(k == 0), stop=False)
                    pe.matmul(out_ap, w[0], x_t[:, 1, k, o:o + n], start=False, stop=False)
                    ins = pe.matmul(out_ap, w[1], x_t[:, 0, k, o:o + n], start=False, stop=(k == nk - 1))
                    if last and k < nk - 1:
                        ins.then_inc(w_used, 1)
                ins.then_inc(acc_full, 1)

            def denominator(i):
                f, c = divmod(i, 3)
                o, n = CHUNKS[c]
                for j in range(2):
                    wait_read(pe, UNIT["z", j])
                pe.wait_ge(st_ready, 2)
                pe.wait_ge(phiq_ready, i + 1)
                if i >= 2:
                    pe.wait_ge(den_read, i - 1)
                pe.matmul(PS[:, 3 + i % 2, 0:n], zblk[:, f, :], phiq[:, f % 2, o:o + n],
                          start=True, stop=True).then_inc(den_done, 1)

            for i in range(24):
                f, c = divmod(i, 3)
                gemm_cols(UNIT["q", f, c], f % 4, c, Q0 + KD * (f // 4), KD, act_t, f % 4 == 0 and c == 0,
                          f % 4 == 3 and c == 2)
                if i >= 3:
                    denominator(i - 3)
                around(40 + i)
            pe_big = None
            for half in range(2):
                for t in range(NT):
                    u = UNIT["h", half, t]
                    gemm_rows(u, t, G0 + KD * half, t == 0, t == NT - 1)
                    if half == 0 and t < 3:
                        denominator(21 + t)
                if half:
                    for p in range(KD):
                        u = UNIT["m", 0, p]
                        b = open_unit(u)
                        pe.wait_ge(st_ready, 2)
                        pe.wait_ge(wo_in[p % 2], 16 * (p // 2 + 1))
                        pe.matmul(PS[:, b, :], st_blk[:, p, :], wo_sb[:, p % 2, :], start=True, stop=True).then_inc(acc_full, 1)
                else:
                    pe.wait_ge(big_ready, 1)
                    pe_big = pe.value_load(big_i[0:1, 0:1], min_val=0, max_val=2 * E)
                for t in range(NT):
                    i = NT * half + t
                    u = UNIT["agg", half, t]
                    b = open_unit(u)
                    out_ap = PS[0:rows(t), b, :]
                    pe.wait_ge(cf_ready, i + 1)
                    if t == 0:
                        for j in range(NT):
                            wait_read(pe, UNIT["h", half, j])
                    for st in range(NT):
                        lhs = cf[0:rows(st), i % 2, st, 0:rows(t)]
                        pe.matmul(out_ap, lhs, hs[0:rows(st), 0, st, :], start=(st == 0), stop=False)
                        if st < NT - 1:
                            pe.matmul(out_ap, lhs, hs[0:rows(st), 1, st, :], start=False, stop=False)
                    with pe.If(pe_big > EXACT_COUNT):
                        pe.wait_ge(clo_ready, i + 1)
                        for st in range(NT):
                            for hl in range(2):
                                pe.matmul(out_ap, clo[0:rows(st), st, 0:rows(t)], hs[0:rows(st), hl, st, :],
                                          start=False, stop=False)
                    st = NT - 1
                    pe.matmul(out_ap, cf[0:rows(st), i % 2, st, 0:rows(t)], hs[0:rows(st), 1, st, :],
                              start=False, stop=True).then_inc(acc_full, 1)

            def mix(half, t):
                u = UNIT["mix", half, t]
                b = open_unit(u)
                out_ap = PS[0:rows(t), b, :]
                for k in range(KD):
                    m = [m1[:, hl, k, :] if half else ring[:, slot(M0 + k), hl, :] for hl in range(2)]
                    pe.matmul(out_ap, node_rows(0, k, t), m[0], start=(k == 0), stop=False)
                    pe.matmul(out_ap, node_rows(1, k, t), m[0], start=False, stop=False)
                    ins = pe.matmul(out_ap, node_rows(0, k, t), m[1], start=False, stop=(k == KD - 1))
                    if half == 0 and t == NT - 1 and k < KD - 1:
                        ins.then_inc(w_used, 1)
                ins.then_inc(acc_full, 1)

            pe.wait_ge(ph_lo, 2 * KD)
            for p in range(KD):
                wait_read(pe, UNIT["m", 0, p])
            for t in range(NT):
                if t == 2:
                    for p in range(KD):
                        u = UNIT["m", 1, p]
                        b = open_unit(u)
                        pe.wait_ge(wo_in[p % 2], 16 * ((KD + p) // 2 + 1))
                        pe.matmul(PS[:, b, :], st_blk[:, p, :], wo_sb[:, p % 2, :], start=True, stop=True).then_inc(acc_full, 1)
                mix(0, t)
            for p in range(KD):
                wait_read(pe, UNIT["m", 1, p])
            for t in range(NT + 2):
                if t < NT:
                    mix(1, t)
                if t >= 2:
                    transpose_tile(NT + t - 2)
            pe.wait_ge(tr_lo, 4 * NT)
            for f, c in GATED:
                k0 = A0 if f < 2 else B0
                gemm_cols(UNIT["a", f, c], f % 2, c, k0, KD, act_t, f % 2 == 0 and c == 0, False)
                gemm_cols(UNIT["b", f, c], 2 + f % 2, c, k0, KD, act_t, False, f % 2 == 1 and c == 2)
            for g in range(2):
                for c in range(3):
                    if g == 0:
                        pe.wait_ge(hid_lo, 6 + 2 * (c + 1))
                    else:
                        pe.wait_ge(g_lo, KH * (c + 1))
                    for f in range(KH):
                        gemm_cols(UNIT[("g1", "g2")[g], f, c], f, c, (C0, D0)[g], KH, act_t if g else hid_t,
                                  c == 0 and f == 0, c == 2 and f == KH - 1)
            pe.wait_ge(g_lo, 24)
            for t in range(NT):
                for h in range(2):
                    u = UNIT["y", t, h]
                    b = open_unit(u)
                    out_ap = PS[0:rows(t), b, :]
                    for k in range(KH):
                        s = slot(E0 + KH * h + k)
                        if t == 0:
                            pe.wait_ge(w_ready, slice_ready(E0 + KH * h + k))
                        lhs = [hid_t[:, hl, k, t * P:t * P + rows(t)] for hl in range(2)]
                        pe.matmul(out_ap, lhs[0], ring[:, s, 0, :], start=(k == 0), stop=False)
                        pe.matmul(out_ap, lhs[1], ring[:, s, 0, :], start=False, stop=False)
                        ins = pe.matmul(out_ap, lhs[0], ring[:, s, 1, :], start=False, stop=(k == KH - 1))
                    ins.then_inc(acc_full, 1)


_OUT = ((N, D), "float32")


def kernel(**inputs):
    import numpy as np
    import concourse.bacc as _bacc
    from concourse.bass_utils import run_bass_kernel_spmd as _run

    g = {k: np.asarray(v) for k, v in inputs.items()}
    wk, wv, wq, wo = (g[f"L0_mix_W{c}"].T for c in "kvqo")
    kv = [np.concatenate([wk[:, 256 * s:256 * s + 256], wv[:, 256 * s:256 * s + 256]], 1) for s in range(4)]
    slabs = kv + [wq[:, :512], wq[:, 512:], g["L0_gnn_W"][:, :512], g["L0_gnn_W"][:, 512:]]
    w3 = g["L0_ffn_w3_w"].T
    w1, w2 = g["L0_ffn_w1_w"].T, g["L0_ffn_w2_w"].T
    slabs += [np.concatenate([w1[:, 256 * s:256 * s + 256], w2[:, 256 * s:256 * s + 256]], 1) for s in range(2)]
    slabs += [g["L0_ffn_h1_w"].T, g["L0_ffn_h2_w"].T, w3[:, :512], w3[:, 512:]]
    wslices = np.concatenate([s.reshape(-1, P, 512) for s in slabs])
    src = np.zeros(NCH_PAD * P, np.int32)
    dst = np.full(NCH_PAD * P, NEVER, np.int32)
    src[:E] = g["src"]
    dst[:E] = g["dst"]
    bk, bv = g["L0_mix_bk"], g["L0_mix_bv"]
    a = {
        "x": g["x"],
        "src_cols": src.reshape(NCH_PAD, P).T,
        "dst_cols": dst.reshape(NCH_PAD, P).T,
        "dst_rows": dst[:ROWS_P * ROWS_T * P].reshape(ROWS_P, ROWS_T, P),
        "wslices": wslices,
        "wo": wo.reshape(KD, P, D),
        "bkv": np.stack([np.concatenate([bk[256 * s:256 * s + 256], bv[256 * s:256 * s + 256]]) for s in range(4)]),
        "bq": g["L0_mix_bq"].reshape(KD, P).T,
        "gb": g["L0_gnn_b"].reshape(1, D),
        "bo": g["L0_mix_bo"].reshape(1, D),
        "scales": np.stack([g[f"L0_ffn_{n}_s"].reshape(KH, P).T for n in ("w1", "w2", "h1", "h2")], 1),
        "w3s": g["L0_ffn_w3_s"].reshape(1, D),
    }
    nc = _bacc.Bacc("TRN2", target_bir_lowering=False, num_devices=1)
    arrays, args = {}, []
    for name, v in a.items():
        v = np.ascontiguousarray(v)
        arrays[f"in_{name}_dram"] = v
        args.append(nc.dram_tensor(f"in_{name}_dram", v.shape, mybir.dt.from_np(v.dtype), kind="ExternalInput").ap())
    args.append(nc.dram_tensor("out_0_dram", _OUT[0], F32, kind="ExternalOutput").ap())
    build(nc, *args)
    r = _run(nc, [arrays], core_ids=[0])
    return r.results[0]["out_0_dram"]
```
